# Optimizing a Trainium2 kernel written in Bass

```python
import numpy as np
import jax
import jax.numpy as jnp

def _softmax(x, axis=-1):
    return jax.nn.softmax(x, axis=axis)

def _gelu(x):
    return jax.nn.gelu(x, approximate=True)

def _silu(x):
    return jax.nn.silu(x)

def _sigmoid(x):
    return jax.nn.sigmoid(x)

def _layernorm(x, axis=-1, eps=1e-05):
    m = jnp.mean(x, axis=axis, keepdims=True)
    v = jnp.var(x, axis=axis, keepdims=True)
    return (x - m) / jnp.sqrt(v + eps)

def _scatter_add(tgt, idx, src, axis=0):
    return tgt.at[idx].add(src)

def _segment_sum(src, seg, n):
    return jax.ops.segment_sum(src, seg, n)
kernel_name = 'mk_seq_preln_d1_jaxref_r8_60cff7'

def setup_inputs(seed: int=0):
    np.random.seed(seed)
    _w = jnp.asarray

    def _L0_attn_setup():
        import jax, jax.numpy as jnp
        import numpy as np
        D_MODEL, D_STATE, BATCH, SEQ_LEN = (128, 64, 4, 512)
        key = jax.random.key(seed)
        k1, k2, k3, k4 = jax.random.split(key, 4)
        x = jax.random.normal(k1, (BATCH, SEQ_LEN, D_MODEL), dtype=jnp.float32)
        A = jax.random.normal(k2, (D_STATE, D_STATE), dtype=jnp.float32) * 0.01
        B = jax.random.normal(k3, (D_STATE, D_MODEL), dtype=jnp.float32) * 0.01
        C = jax.random.normal(k4, (D_MODEL, D_STATE), dtype=jnp.float32) * 0.01
        D = jnp.ones((D_MODEL,), dtype=jnp.float32)
        return {'x': x, 'A': A, 'B': B, 'C': C, 'D': D}
    _L0_attn_in = _L0_attn_setup()

    def _L0_ffn_setup():
        import jax, jax.numpy as jnp
        import numpy as np
        B, S, H, F, E = (1, 256, 128, 256, 8)

        def _swiglu(x, wg, wu, wd):
            return jax.nn.silu(x @ wg.T) * (x @ wu.T) @ wd.T
        key = jax.random.key(seed)
        ks = jax.random.split(key, 8)
        sc = 1.0 / np.sqrt(H)
        scf = 1.0 / np.sqrt(F)
        return {'hidden_states': jax.random.normal(ks[0], (B, S, H), jnp.float32), 'gate_w': jax.random.normal(ks[1], (E, H), jnp.float32) * sc, 'shared_gate': jax.random.normal(ks[2], (F, H), jnp.float32) * sc, 'shared_up': jax.random.normal(ks[3], (F, H), jnp.float32) * sc, 'shared_down': jax.random.normal(ks[4], (H, F), jnp.float32) * scf, 'r_gate': jax.random.normal(ks[5], (E, F, H), jnp.float32) * sc, 'r_up': jax.random.normal(ks[6], (E, F, H), jnp.float32) * sc, 'r_down': jax.random.normal(ks[7], (E, H, F), jnp.float32) * scf}
    _L0_ffn_in = _L0_ffn_setup()
    _d = {'L0_attn_x': _L0_attn_in['x'], 'L0_attn_A': _L0_attn_in['A'], 'L0_attn_B': _L0_attn_in['B'], 'L0_attn_C': _L0_attn_in['C'], 'L0_attn_D': _L0_attn_in['D'], 'L0_ffn_gate_w': _L0_ffn_in['gate_w'], 'L0_ffn_shared_gate': _L0_ffn_in['shared_gate'], 'L0_ffn_shared_up': _L0_ffn_in['shared_up'], 'L0_ffn_shared_down': _L0_ffn_in['shared_down'], 'L0_ffn_r_gate': _L0_ffn_in['r_gate'], 'L0_ffn_r_up': _L0_ffn_in['r_up'], 'L0_ffn_r_down': _L0_ffn_in['r_down']}
    _x0 = _d['L0_attn_x']
    _d['L0_attn_x'] = jax.random.normal(jax.random.fold_in(jax.random.key(seed), 1), (16, 512, 128), dtype=_x0.dtype)
    del _x0
    return _d

def reference(L0_attn_x, L0_attn_A, L0_attn_B, L0_attn_C, L0_attn_D, L0_ffn_gate_w, L0_ffn_shared_gate, L0_ffn_shared_up, L0_ffn_shared_down, L0_ffn_r_gate, L0_ffn_r_up, L0_ffn_r_down):

    def _L0_attn_ref(x, A, B, C, D):
        import jax, jax.numpy as jnp
        import numpy as np
        D_MODEL, D_STATE, BATCH, SEQ_LEN = (128, 64, 4, 512)
        a = jnp.diagonal(A)
        Bu = jnp.einsum('sd,bld->lbs', B, x)

        def step(h, bu_t):
            h = a * h + bu_t
            return (h, h)
        h0 = jnp.zeros((x.shape[0], a.shape[0]), dtype=x.dtype)
        _, hs = jax.lax.scan(step, h0, Bu)
        y = jnp.einsum('ds,lbs->bld', C, hs) + D * x
        return y

    def _L0_ffn_ref(hidden_states, gate_w, shared_gate, shared_up, shared_down, r_gate, r_up, r_down):
        import jax, jax.numpy as jnp
        import numpy as np
        B, S, H, F, E = (1, 256, 128, 256, 8)

        def _swiglu(x, wg, wu, wd):
            return jax.nn.silu(x @ wg.T) * (x @ wu.T) @ wd.T
        b, s, h = hidden_states.shape
        x = hidden_states.reshape(-1, h)
        shared_out = _swiglu(x, shared_gate, shared_up, shared_down)
        logits = x @ gate_w.T
        top_id = jnp.argmax(logits, axis=-1)
        score = jax.nn.sigmoid(jnp.max(logits, axis=-1))
        xs = x * score[:, None]

        def body(acc, ws):
            wg, wu, wd, e = ws
            xe = jnp.where((top_id == e)[:, None], xs, 0.0)
            return (acc + _swiglu(xe, wg, wu, wd), None)
        acc0 = jnp.zeros_like(x)
        routed_out, _ = jax.lax.scan(body, acc0, (r_gate, r_up, r_down, jnp.arange(E)))
        return (shared_out + routed_out).reshape(b, s, h)
    x = L0_attn_x
    x = x + _L0_attn_ref(_layernorm(x, axis=-1), L0_attn_A, L0_attn_B, L0_attn_C, L0_attn_D)
    x = x + _L0_ffn_ref(_layernorm(x, axis=-1), L0_ffn_gate_w, L0_ffn_shared_gate, L0_ffn_shared_up, L0_ffn_shared_down, L0_ffn_r_gate, L0_ffn_r_up, L0_ffn_r_down)
    return x

_drawn_inputs = setup_inputs


def setup_inputs(seed=0):
    import zlib

    import numpy as np

    out = dict(_drawn_inputs(seed))
    spreads = {'L0_attn_D': (1.0, 0.2)}
    factors = {'L0_attn_A': 35.827, 'L0_attn_B': 4.788, 'L0_attn_C': 4.686}
    for name, (base, spread) in spreads.items():
        noise = np.random.default_rng([zlib.crc32(name.encode()), seed]).standard_normal(out[name].shape)
        drawn = base * np.exp(spread * noise) if base else spread * noise
        out[name] = jnp.asarray(drawn.astype(out[name].dtype))
    for name, factor in factors.items():
        out[name] = (out[name] * factor).astype(out[name].dtype)
    return out
```

```python
from contextlib import ExitStack

import numpy as np

import concourse.bass as bass
from concourse import mybir

P = 128
F32 = mybir.dt.float32
F16 = mybir.dt.float16
I32 = mybir.dt.int32
ALU = mybir.AluOpType
ACT = mybir.ActivationFunctionType
AX = mybir.AxisListType.X
MAX_OF_PARTITIONS = bass.bass_isa.ReduceOp.max

SLOTS = 256
BIG_EXPONENT = 0x7F800000
LN_EPS = 1e-5
X_SCALE = 256.0
W_SCALE = 1024.0
H_SCALE = 0.25
ROUTER, GATE, UP, DOWN = range(4)


PLACE_STEPS = 18


def run_pairs(engine, pairs, step, between=None):
    def peeled(p):
        step(p, lambda k: 0 <= p + k < pairs)

    for p in range(-2, 2):
        peeled(p)
    if between:
        between()
    with engine.Fori(2, pairs - 2) as p:
        step(p, lambda k: True)
    for p in range(pairs - 2, pairs + 1):
        peeled(p)


def run_blocks(engine, blocks, step):
    def peeled(b):
        step(b, b % 4, b // 4, lambda k: 0 <= b + k < blocks)

    for b in range(8):
        peeled(b)
    with engine.Fori(2, blocks // 4) as i:
        for k in range(4):
            step(i * 4 + k, k, i, lambda m: True)
    peeled(blocks)


def run_tiles(engine, tiles, step):
    def peeled(j):
        step(j, j % 3, j // 3, lambda k: 0 <= j + k < tiles)

    for j in range(-1, 6):
        peeled(j)
    with engine.Fori(2, tiles // 3 - 1) as i:
        for k in range(3):
            step(i * 3 + k, k, i, lambda m: True)
    for j in range(tiles - 3, tiles + 2):
        peeled(j)


def after(engine, semaphore, count):
    if isinstance(count, int) and count <= 0:
        return
    engine.wait_ge(semaphore, count)


def block_kernel(nc, x, bT, cT, a_diag, d_row, gateT, weights, consts, tri_ones, token_ids, out):
    BATCH, SEQ, D = x.shape
    N = bT.shape[1]
    E = gateT.shape[1]
    EW = E + 1
    F = weights.shape[2] // EW
    FC = F // P
    T = BATCH * SEQ
    NT = T // P
    BT = SEQ // P
    PT = 2 * BT
    PAIRS = BATCH // 2
    BLOCKS = BATCH
    TILES = T // SLOTS + E - 1
    SH = SLOTS // P
    ROW = 2 * D + 8
    assert D == P and N * 2 == P and FC == 2 and SH == 2 and TILES % 3 == 0 and SEQ == 512

    table = nc.dram_tensor("table", (TILES * SLOTS, ROW), F32, kind="Internal").ap()

    with ExitStack() as ctx:
        def sb(name, shape, dtype=F32):
            return ctx.enter_context(nc.sbuf_tensor(name, shape, dtype))

        def sem(name):
            return ctx.enter_context(nc.semaphore(name))

        x1 = sb("x1", [P, NT, D])
        n2 = sb("n2", [P, NT, D])
        n2T_hi = sb("n2T_hi", [P, T], F16)
        n2T_lo = sb("n2T_lo", [P, T], F16)
        w_split = sb("w_split", [P, 3, EW, 2, F], F16)
        router_f = sb("router_f", [P, E])
        router_split = sb("router_split", [P, 2, E], F16)
        identity = sb("identity", [P, P])
        expert_less_E = sb("expert_less_E", [P, E])
        segment_mask = sb("segment_mask", [P, E * NT])
        tile_number = sb("tile_number", [P, TILES])
        tri = sb("tri", [P, P], F16)
        ones = sb("ones", [P, P], F16)
        ids = sb("ids", [P, NT], I32)
        b_w = sb("b_w", [P, N])
        c_w = sb("c_w", [P, D])
        a_col = sb("a_col", [P, 1])
        d_bc = sb("d_bc", [P, D])
        eps1 = sb("eps1", [P, 1])
        eps2 = sb("eps2", [P, 1])
        w_max = sb("w_max", [P, 4])
        w_top = sb("w_top", [P, 4])
        w_pow = sb("w_pow", [P, 4])
        w_inv = sb("w_inv", [P, 4])
        w_mul = sb("w_mul", [P, 4])
        g_scale = sb("g_scale", [P, 1])
        l_scale = sb("l_scale", [P, 1])
        h_scale = sb("h_scale", [P, 1])
        o_scale = sb("o_scale", [P, 3])
        stats1 = sb("stats1", [P, PT, 6])
        mv1 = sb("mv1", [P, PT, 2])
        sd1 = sb("sd1", [P, PT])
        r1 = sb("r1", [P, PT])
        n1 = sb("n1", [P, PT, D])
        n1T = [sb(f"n1T{b}", [P, SEQ]) for b in range(2)]
        z = sb("z", [P, PT, D])
        h = sb("h", [P, SEQ])
        n2_new = sb("n2_new", [P, PT, D])
        stats2 = sb("stats2", [P, PT, 6])
        mv2 = sb("mv2", [P, PT, 2])
        sd2 = sb("sd2", [P, PT])
        r2 = sb("r2", [P, PT])
        nb2 = sb("nb2", [P, PT])
        top_logit = sb("top_logit", [P, NT])
        is_top = sb("is_top", [P, PT, E])
        first_top = sb("first_top", [P, PT])
        one_hot = sb("one_hot", [P, NT, E], F16)
        score = sb("score", [P, NT])
        counts = sb("counts", [P, E, NT])
        running = sb("running", [P, E, NT])
        tiles_f = sb("tiles_f", [P, E])
        tiles_i = sb("tiles_i", [P, E], I32)
        end_tile = sb("end_tile", [P, E])
        start_row = sb("start_row", [P, E])
        place_f = sb("place_f", [P, NT])
        place = sb("place", [P, NT], I32)
        wait_taker = sb("wait_taker", [P, 1])
        ended = sb("ended", [P, TILES, E])
        tile_expert_f = sb("tile_expert_f", [P, TILES])
        tile_weights = sb("tile_weights", [P, TILES], I32)
        row_place = [sb(f"row_place{k}", [P, BT], I32) for k in range(4)]
        pad_row = sb("pad_row", [P, ROW])
        halves = [t[:, BT * b:BT * (b + 1), :].rearrange("p t d -> p (t d)") for t in (n1, z) for b in range(2)]
        silu = [halves[0], halves[1], n1T[0][:]]
        hid = [halves[2], halves[3], n1T[1][:]]
        hid_hi = [sb(f"hid_hi{k}", [P, SEQ], F16) for k in range(4)]
        hid_lo = [sb(f"hid_lo{k}", [P, SEQ], F16) for k in range(4)]
        w_full = sb("w_full", [P, 3, EW * F])
        x_in = [w_full[:, 0, SLOTS * k:SLOTS * (k + 1)].rearrange("p (s d) -> p s d", s=SH) for k in range(3)]
        result = [w_full[:, 0, SLOTS * (3 + k):SLOTS * (4 + k)].rearrange("p (s d) -> p s d", s=SH) for k in range(3)]
        BW = SH * (ROW - D)
        base_in = [w_full[:, 1, BW * k:BW * (k + 1)].rearrange("p (s r) -> p s r", s=SH) for k in range(3)]
        rows = [sb(f"rows{k}", [P, BT, ROW]) for k in range(2)] + [
            w_full[:, 2, BT * ROW * k:BT * ROW * (k + 1)].rearrange("p (t r) -> p t r", t=BT) for k in range(2)]
        result_id = [sb(f"result_id{k}", [P, SH], I32) for k in range(3)]
        xT_hi = [sb(f"xT_hi{k}", [P, SLOTS], F16) for k in range(3)]
        xT_lo = [sb(f"xT_lo{k}", [P, SLOTS], F16) for k in range(3)]
        bank = [ctx.enter_context(nc.psum_tensor(f"bank{k}", [P, 512], F32)) for k in range(8)]

        s_small, s_router = sem("small_loaded"), sem("router_loaded")
        s_x = [sem(f"x_loaded{q}") for q in range(PAIRS)]
        s_w = sem("weights_loaded")
        s_eps = sem("eps_set")
        s_const = sem("constants_loaded")
        s_rlo = sem("router_lo_ready")
        s_pad_row = sem("pad_row_set")
        s_padded = sem("table_padded")
        s_wmax = sem("weight_max_ready")
        s_wtop = sem("weight_top_ready")
        s_scale = sem("scale_steps")
        s_whi = sem("weights_hi")
        s_wlo, s_wmul, s_wlo_routed = sem("shared_weights_lo"), sem("weights_scaled"), sem("routed_weights_lo")
        s_bn1, s_mv1, s_sd1, s_r1 = sem("stats1_done"), sem("mv1_ready"), sem("sd1_ready"), sem("r1_ready")
        s_n1, s_t1, s_n1T, s_bu = sem("n1_ready"), sem("n1_transposed"), sem("n1T_ready"), sem("bu_ready")
        s_h, s_y, s_zm, s_z, s_x1 = sem("h_ready"), sem("y_ready"), sem("d_n1_ready"), sem("z_ready"), sem("x1_ready")
        s_bn2, s_mv2, s_sd2 = sem("stats2_done"), sem("mv2_ready"), sem("sd2_ready")
        s_kept = sem("n2_kept")
        s_r2, s_nb2, s_n2 = sem("r2_ready"), sem("nb2_ready"), sem("n2_ready")
        s_t2, s_hi, s_lo = sem("n2_transposed"), sem("n2T_hi_ready"), sem("n2T_lo_ready")
        s_logit, s_route = sem("logits_ready"), sem("route_steps")
        s_rank, s_score, s_place = sem("ranks_ready"), sem("score_ready"), sem("place_steps")
        s_g, s_u, s_silu, s_hid = sem("sh_gate"), sem("sh_up"), sem("sh_silu"), sem("sh_hidden")
        s_hh, s_hl, s_o = sem("sh_hidden_hi"), sem("sh_hidden_lo"), sem("sh_down")
        s_xs, s_base = sem("row_input_ready"), sem("row_base_ready")
        s_scattered = [sem(f"rows_scattered{k}") for k in range(4)]
        s_xin = [sem(f"tile_input_loaded{k}") for k in range(3)]
        s_bin = [sem(f"tile_base_loaded{k}") for k in range(3)]
        s_xt, s_xh, s_xl = sem("tile_transposed"), sem("tile_hi"), sem("tile_lo")
        r_g, r_u, r_silu, r_hid = sem("ro_gate"), sem("ro_up"), sem("ro_silu"), sem("ro_hidden")
        r_hh, r_hl, r_o, r_out = sem("ro_hidden_hi"), sem("ro_hidden_lo"), sem("ro_down"), sem("result_ready")
        s_stored = [sem(f"result_stored{k}") for k in range(3)]

        SMALL = 10
        ROUTE = 5

        x_tiles = x.rearrange("b (t p) d -> p (b t) d", p=P)
        out_rows = out.rearrange("b s d -> (b s) d")
        table_x = table[:, 0:D].rearrange("(j p s) d -> j p s d", p=P, s=SH)
        table_base = table[:, D:ROW].rearrange("(j p s) r -> j p s r", p=P, s=SH)

        block = ctx.enter_context(nc.Block())

        @block.sync
        def _(sp):
            sp.dma_start(x1[:, 0:PT, :], x_tiles[:, 0:PT, :]).then_inc(s_x[0], 16)
            sp.dma_start(router_f[:], gateT).then_inc(s_router, 16)
            for dst, src in ((b_w[:], bT), (c_w[0:N, :], cT), (c_w[N:P, :], cT), (a_col[0:N, :], a_diag),
                             (a_col[N:P, :], a_diag), (d_bc[:], d_row.to_broadcast([P, D])),
                             (tri[:], tri_ones[:, 0:P]), (ones[:], tri_ones[:, P:2 * P])):
                sp.dma_start(dst, src).then_inc(s_small, 16)
            c0 = 0
            sp.dma_start(ids[:], token_ids).then_inc(s_small, 16)
            for dst in (identity, expert_less_E, segment_mask, tile_number):
                width = dst.shape[1]
                s = s_small if dst is identity else s_const
                sp.dma_start(dst[:], consts[:, c0:c0 + width]).then_inc(s, 16)
                c0 += width
            sp.dma_start(x1[:, PT:2 * PT, :], x_tiles[:, PT:2 * PT, :]).then_inc(s_x[1], 16)
            for k in range(3):
                sp.dma_start(w_full[:, k, :], weights[k]).then_inc(s_w, 16)
            for q in range(2, PAIRS):
                sp.dma_start(x1[:, PT * q:PT * (q + 1), :], x_tiles[:, PT * q:PT * (q + 1), :]).then_inc(s_x[q], 16)

            def keep_n2(q):
                sp.wait_ge(s_n2, q * 2 + 2)
                sp.dma_start(n2[:, bass.ds(q * PT, PT), :], n2_new[:]).then_inc(s_kept, 16)

            PIECES = 6
            GROUPS = TILES * SH // PIECES

            def pad_table(piece):
                dst = table[bass.ds(piece * (GROUPS * P), GROUPS * P), :].rearrange("(n p) r -> p n r", p=P)
                sp.dma_start(dst, pad_row[:, None, :].to_broadcast([P, GROUPS, ROW])).then_inc(s_padded, 16)

            sp.wait_ge(s_pad_row, 2)
            run_pairs(sp, PAIRS, lambda p, has: (
                has(0) and keep_n2(p),
                has(0) and has(2) and pad_table(p)))

            sp.wait_ge(s_wlo_routed, 3)
            for k in range(4):
                sp.wait_ge(s_scattered[k], 16 * BT * BLOCKS // 4)

            def load_input(j, k):
                after(sp, s_xt, j - 2)
                sp.dma_start(x_in[k], tile_of(table_x, j)).then_inc(s_xin[k], 16)

            def load_base(j, k):
                after(sp, r_out, j - 2)
                sp.dma_start(base_in[k], tile_of(table_base, j)).then_inc(s_bin[k], 16)

            def tile_of(view, j):
                return view[bass.ds(j, 1)].rearrange("o p s r -> (o p) s r")

            def load_step(j, k, turn, has):
                has(0) and load_input(j, k)
                has(-2) and load_base(j - 2, (k - 2) % 3)

            run_tiles(sp, TILES, load_step)
            for k in range(3):
                sp.wait_ge(s_stored[k], 16 * SH * (TILES // 3))

        @block.tensor
        def _(pe):
            mm = nc.tensor.matmul

            def transpose_n1(q):
                for b in range(2):
                    pe.wait_ge(s_n1, q * 2 + b + 1)
                    after(pe, s_n1T, q * 2 + (b - 1))
                    for t in range(BT):
                        last = nc.tensor.transpose(bank[b][:, P * t:P * (t + 1)], n1[:, BT * b + t, :], identity[:])
                    last.then_inc(s_t1, 1)

            def bu(q):
                pe.wait_ge(s_n1T, q * 2 + 2)
                after(pe, s_h, q)
                for b in range(2):
                    last = mm(bank[2][N * b:N * (b + 1), :], b_w[:], n1T[b][:], start=True, stop=True)
                last.then_inc(s_bu, 1)

            def y(q):
                pe.wait_ge(s_h, q + 1)
                for b in range(2):
                    after(pe, s_x1, q * 2 + (b - 1))
                    for t in range(BT):
                        last = mm(bank[3 + b][:, P * t:P * (t + 1)], h[N * b:N * (b + 1), P * t:P * (t + 1)],
                                  c_w[N * b:N * (b + 1), :], start=True, stop=True)
                    last.then_inc(s_y, 1)

            def transpose_n2(q):
                for b in range(2):
                    pe.wait_ge(s_n2, q * 2 + b + 1)
                    after(pe, s_lo, q * 2 + (b - 1))
                    for t in range(BT):
                        last = nc.tensor.transpose(bank[5 + b][:, P * t:P * (t + 1)], n2_new[:, BT * b + t, :], identity[:])
                    last.then_inc(s_t2, 1)

            def logits(q):
                if isinstance(q, int) and q == 0:
                    pe.wait_ge(s_rlo, 1)
                pe.wait_ge(s_lo, q * 2 + 2)
                after(pe, s_route, q * ROUTE - ROUTE + 2)
                for t in range(PT):
                    tok = bass.ds(q * (PT * P) + t * P, P)
                    o = bank[7][:, E * t:E * (t + 1)]
                    mm(o, n2T_hi[:, tok], router_split[:, 0, :], start=True, stop=False)
                    mm(o, n2T_hi[:, tok], router_split[:, 1, :], start=False, stop=False)
                    last = mm(o, n2T_lo[:, tok], router_split[:, 0, :], start=False, stop=True)
                last.then_inc(s_logit, 1)

            pe.wait_ge(s_small, 16 * SMALL)
            run_pairs(pe, PAIRS, lambda p, has: (
                has(0) and y(p),
                has(1) and transpose_n1(p + 1),
                has(-1) and logits(p - 1),
                has(1) and bu(p + 1),
                has(0) and transpose_n2(p)))

            pe.wait_ge(s_route, ROUTE * PAIRS)
            hot = one_hot[:].rearrange("p t e -> p (t e)")
            mm(bank[0][:], tri[:], hot, start=True, stop=True)
            mm(bank[1][:], ones[:], hot, start=True, stop=True).then_inc(s_rank, 1)

            def shared_gate_up(b):
                tok = bass.ds(b * SEQ, SEQ)
                for c in range(FC):
                    f = slice(P * c, P * (c + 1))
                    for kind, first_bank, used, done in ((0, 2, s_silu, s_g), (1, 4, s_hid, s_u)):
                        after(pe, used, b * FC + (c - FC + 1))
                        o = bank[first_bank + c][:]
                        mm(o, w_split[:, kind, 0, 0, f], n2T_hi[:, tok], start=True, stop=False)
                        mm(o, w_split[:, kind, 0, 0, f], n2T_lo[:, tok], start=False, stop=False)
                        mm(o, w_split[:, kind, 0, 1, f], n2T_hi[:, tok], start=False, stop=True).then_inc(done, 1)

            def shared_down(b, k):
                par = k % 2
                pe.wait_ge(s_hl, b * FC + FC)
                after(pe, s_base, b - 1)
                for t in range(BT):
                    tok = slice(P * t, P * (t + 1))
                    o = bank[6 + par][:, tok]
                    for c in range(FC):
                        f = slice(P * c, P * (c + 1))
                        hi, lo = hid_hi[2 * par + c][:, tok], hid_lo[2 * par + c][:, tok]
                        mm(o, hi, w_split[:, 2, 0, 0, f], start=(c == 0), stop=False)
                        mm(o, hi, w_split[:, 2, 0, 1, f], start=False, stop=False)
                        last = mm(o, lo, w_split[:, 2, 0, 0, f], start=False, stop=(c == FC - 1))
                last.then_inc(s_o, 1)

            pe.wait_ge(s_wlo, 3)
            run_blocks(pe, BLOCKS, lambda b, k, turn, has: (
                has(0) and shared_gate_up(b),
                has(-1) and shared_down(b - 1, (k - 1) % 4)))

            def transpose_tile(j, k, turn):
                pe.wait_ge(s_xin[k], turn * 16 + 16)
                after(pe, s_xl, j)
                for s in range(SH):
                    last = nc.tensor.transpose(bank[0][:, P * s:P * (s + 1)], x_in[k][:, s, :], identity[:])
                last.then_inc(s_xt, 1)

            def routed_gate_up(j, k, e, xT_awaited):
                if not xT_awaited:
                    pe.wait_ge(s_xl, j + 1)
                for kind, first_bank, done in ((0, 1, r_g), (1, 4, r_u)):
                    for c in range(FC):
                        o = bank[first_bank + k][:, SLOTS * c:SLOTS * (c + 1)]
                        w_hi = w_of(kind, e, 0, c)
                        mm(o, w_hi, xT_hi[k][:], start=True, stop=False)
                        mm(o, w_hi, xT_lo[k][:], start=False, stop=False)
                        last = mm(o, w_of(kind, e, 1, c), xT_hi[k][:], start=False, stop=True)
                    last.then_inc(done, 1)

            def w_of(kind, e, part, c):
                return w_flat[:, bass.ds(e + ((kind * EW) * 2 + part) * F + P * c, P)]

            w_flat = w_split[:].rearrange("p k e h f -> p (k e h f)")

            def routed_down(j, k, e):
                pe.wait_ge(r_hl, j + 1)
                after(pe, r_out, j)
                for s in range(SH):
                    o = bank[7][:, P * s:P * (s + 1)]
                    for c in range(FC):
                        slot = slice(SLOTS * c + P * s, SLOTS * c + P * (s + 1))
                        mm(o, hid_hi[k][:, slot], w_of(2, e, 0, c), start=(c == 0), stop=False)
                        mm(o, hid_hi[k][:, slot], w_of(2, e, 1, c), start=False, stop=False)
                        last = mm(o, hid_lo[k][:, slot], w_of(2, e, 0, c), start=False, stop=(c == FC - 1))
                last.then_inc(r_o, 1)

            expert_reg = [nc.tensor.alloc_register(f"expert{k}") for k in range(3)]

            def load_expert(j, k):
                nc.tensor.reg_load(expert_reg[k], tile_weights[0:1, bass.ds(j, 1)])

            def expert(k):
                return nc.tensor.snap(expert_reg[k], min_val=0, max_val=E * 2 * F)

            pe.wait_ge(s_place, PLACE_STEPS)
            pe.wait_ge(s_wlo_routed, 3)
            pe.wait_ge(s_base, BLOCKS)
            run_tiles(pe, TILES, lambda j, k, turn, has: (
                has(1) and transpose_tile(j + 1, (k + 1) % 3, turn + (k + 1) // 3),
                has(0) and routed_gate_up(j, k, expert(k), has(1)),
                has(-2) and routed_down(j - 2, (k - 2) % 3, expert((k - 2) % 3)),
                has(1) and load_expert(j + 1, (k + 1) % 3)))

        @block.scalar
        def _(act):
            run = nc.scalar.activation

            def std1(q):
                act.wait_ge(s_mv1, q + 1)
                run(sd1[:], mv1[:, :, 1], ACT.Sqrt, bias=eps1[:, 0:1]).then_inc(s_sd1, 1)

            def std2(q):
                act.wait_ge(s_mv2, q + 1)
                run(sd2[:], mv2[:, :, 1], ACT.Sqrt, bias=eps2[:, 0:1], scale=X_SCALE ** -2).then_inc(s_sd2, 1)

            def copy_n1T(q):
                for b in range(2):
                    act.wait_ge(s_t1, q * 2 + b + 1)
                    after(act, s_bu, q)
                    run(n1T[b][:], bank[b][:], ACT.Copy).then_inc(s_n1T, 1)

            def norm2(q):
                after(act, s_t2, q * 2)
                after(act, s_kept, q * 16)
                act.wait_ge(s_nb2, q + 1)
                for t in range(PT):
                    last = run(n2_new[:, t, :], x1[:, bass.ds(q * PT + t, 1), :].rearrange("p o d -> p (o d)"),
                               ACT.Identity, bias=nb2[:, t:t + 1], scale=r2[:, t:t + 1])
                    if t % BT == BT - 1:
                        last.then_inc(s_n2, 1)

            def split_hi(q):
                for b in range(2):
                    act.wait_ge(s_t2, q * 2 + b + 1)
                    run(n2T_hi[:, bass.ds(q * (2 * SEQ) + b * SEQ, SEQ)], bank[5 + b][:], ACT.Copy).then_inc(s_hi, 1)

            act.wait_ge(s_eps, 2)

            def router_hi():
                act.wait_ge(s_scale, 4)
                run(router_split[:, 0, :], router_f[:], ACT.Copy, scale=w_mul[:, 0:1]).then_inc(s_whi, 1)

            def weights_hi(k, experts):
                run(w_split[:, k, experts, 0, :], w_full[:, k, :].rearrange("p (e f) -> p e f", e=EW)[:, experts],
                    ACT.Copy, scale=w_mul[:, 1 + k:2 + k]).then_inc(s_whi, 1)

            def pair_step(p, has):
                has(1) and copy_n1T(p + 1)
                has(0) and std2(p)
                has(0) and norm2(p)
                has(2) and std1(p + 2)
                has(0) and split_hi(p)
                if isinstance(p, int) and p == -1:
                    router_hi()

            run_pairs(act, PAIRS, pair_step, between=lambda: (
                act.wait_ge(s_scale, 10),
                [weights_hi(k, experts) for experts in (slice(0, 1), slice(1, EW)) for k in range(3)]))

            act.wait_ge(s_route, ROUTE * PAIRS)
            run(score[:], top_logit[:], ACT.Sigmoid, scale=l_scale[:, 0:1]).then_inc(s_score, 1)

            def shared_silu(s, c, b):
                act.wait_ge(s_g, s + 1)
                after(act, s_hid, s - 1)
                run(silu[c], bank[2 + c][:], ACT.Silu, scale=g_scale[:, 0:1]).then_inc(s_silu, 1)

            def shared_hi(s, c, b, k):
                par = k % 2
                act.wait_ge(s_hid, s + 1)
                after(act, s_o, b - 1)
                run(hid_hi[2 * par + c][:], hid[c], ACT.Copy).then_inc(s_hh, 1)

            def row_input(b, k, turn):
                after(act, s_scattered[k], turn * (16 * BT))
                for t in range(BT):
                    i = bass.ds(b * BT + t, 1)
                    last = run(rows[k][:, t, 0:D], n2[:, i, :].rearrange("p o d -> p (o d)"), ACT.Copy,
                               scale=score[:, i])
                last.then_inc(s_xs, 1)

            act.wait_ge(s_score, 1)
            act.wait_ge(s_kept, 16 * PAIRS)
            act.wait_ge(s_wlo_routed, 1)
            run_blocks(act, BLOCKS, lambda b, k, turn, has: (
                has(-1) and shared_hi(b * FC - 1, 1, b - 1, (k - 1) % 4),
                has(0) and shared_silu(b * FC, 0, b),
                has(0) and shared_silu(b * FC + 1, 1, b),
                has(0) and shared_hi(b * FC, 0, b, k),
                has(0) and row_input(b, k, turn)))

            def tile_hi(j, k):
                act.wait_ge(s_xt, j + 1)
                after(act, r_u, j - 2)
                run(xT_hi[k][:], bank[0][:, 0:SLOTS], ACT.Copy).then_inc(s_xh, 1)

            def routed_silu(j, k):
                act.wait_ge(r_g, j + 1)
                after(act, r_hid, j - 2)
                run(silu[k], bank[1 + k][:], ACT.Silu, scale=g_scale[:, 0:1]).then_inc(r_silu, 1)

            def routed_hi(j, k):
                act.wait_ge(r_hid, j + 1)
                after(act, r_o, j - 2)
                run(hid_hi[k][:], hid[k], ACT.Copy).then_inc(r_hh, 1)

            run_tiles(act, TILES, lambda j, k, turn, has: (
                has(1) and tile_hi(j + 1, (k + 1) % 3),
                has(-1) and routed_hi(j - 1, (k - 1) % 3),
                has(0) and routed_silu(j, k)))

        @block.vector
        def _(dve):
            v = nc.vector

            def take_wait():
                v.memset(wait_taker[:], 0.0)

            def power_of_two(col, steps_before):
                v.tensor_scalar(w_top[:, col], w_top[:, col], 2.0 ** -60, None, ALU.max).then_inc(s_scale, 1)
                steps_before += 1
                dve.wait_ge(s_scale, steps_before)
                v.tensor_scalar(w_pow[:, col].bitcast(I32), w_top[:, col].bitcast(I32), BIG_EXPONENT, None,
                                ALU.bitwise_and).then_inc(s_scale, 1)
                dve.wait_ge(s_scale, steps_before + 1)
                v.reciprocal(w_inv[:, col], w_pow[:, col]).then_inc(s_scale, 1)
                dve.wait_ge(s_scale, steps_before + 2)
                v.tensor_scalar(w_mul[:, col], w_inv[:, col], W_SCALE, None, ALU.mult).then_inc(s_scale, 1)

            def norm1_stats(q):
                if isinstance(q, int):
                    dve.wait_ge(s_x[q], 16)
                for t in range(PT):
                    last = v.bn_stats(stats1[:, t, :], x1[:, bass.ds(q * PT + t, 1), :].rearrange("p o d -> p (o d)"))
                last.then_inc(s_bn1, 1)
                dve.wait_ge(s_bn1, q + 1)
                take_wait()
                for t in range(PT):
                    last = v.bn_aggr(mv1[:, t, :], stats1[:, t, :])
                last.then_inc(s_mv1, 1)

            def norm1(q):
                dve.wait_ge(s_sd1, q + 1)
                v.reciprocal(r1[:], sd1[:]).then_inc(s_r1, 1)
                dve.wait_ge(s_r1, q + 1)
                after(dve, s_t1, q * 2)
                after(dve, s_z, q)
                for t in range(PT):
                    last = v.tensor_scalar(n1[:, t, :], x1[:, bass.ds(q * PT + t, 1), :].rearrange("p o d -> p (o d)"),
                                           mv1[:, t, 0:1], r1[:, t:t + 1], ALU.subtract, ALU.mult)
                    if t % BT == BT - 1:
                        last.then_inc(s_n1, 1)

            def scan(q):
                dve.wait_ge(s_bu, q + 1)
                after(dve, s_y, q * 2)
                v.tensor_tensor_scan(h[:], a_col[:, 0:1].to_broadcast([P, SEQ]), bank[2][:], 0.0,
                                     ALU.mult, ALU.add).then_inc(s_h, 1)

            def residual(q):
                dve.wait_ge(s_z, q + 1)
                for b in range(2):
                    dve.wait_ge(s_y, q * 2 + b + 1)
                    own = x1[:, bass.ds(q * PT + b * BT, BT), :]
                    v.tensor_tensor(out=own, in0=bank[3 + b][:].rearrange("p (t d) -> p t d", t=BT),
                                    in1=z[:, BT * b:BT * (b + 1), :], op=ALU.add).then_inc(s_x1, 1)
                dve.wait_ge(s_x1, q * 2 + 2)
                take_wait()
                for t in range(PT):
                    last = v.bn_stats(stats2[:, t, :], x1[:, bass.ds(q * PT + t, 1), :].rearrange("p o d -> p (o d)"))
                last.then_inc(s_bn2, 1)
                dve.wait_ge(s_bn2, q + 1)
                take_wait()
                for t in range(PT):
                    last = v.bn_aggr(mv2[:, t, :], stats2[:, t, :])
                last.then_inc(s_mv2, 1)

            def norm2_scales(q):
                dve.wait_ge(s_sd2, q + 1)
                after(dve, s_n2, q * 2)
                v.reciprocal(r2[:], sd2[:]).then_inc(s_r2, 1)
                dve.wait_ge(s_r2, q + 1)
                v.scalar_tensor_tensor(out=nb2[:], in0=mv2[:, :, 0], scalar=-1.0, in1=r2[:], op0=ALU.mult,
                                       op1=ALU.mult).then_inc(s_nb2, 1)

            def split_lo(q):
                for b in range(2):
                    tok = bass.ds(q * (2 * SEQ) + b * SEQ, SEQ)
                    dve.wait_ge(s_hi, q * 2 + b + 1)
                    v.tensor_tensor(out=n2T_lo[:, tok], in0=bank[5 + b][:], in1=n2T_hi[:, tok],
                                    op=ALU.subtract).then_inc(s_lo, 1)

            def route(q):
                step = q * ROUTE
                lg = bank[7][:, 0:PT * E].rearrange("p (t e) -> p t e", t=PT)
                tops = top_logit[:, bass.ds(q * PT, PT)]
                numbers = expert_less_E[:, None, :].to_broadcast([P, PT, E])
                dve.wait_ge(s_logit, q + 1)
                v.tensor_reduce(tops, lg, AX, ALU.max).then_inc(s_route, 1)
                dve.wait_ge(s_route, step + 1)
                v.tensor_tensor(out=is_top[:], in0=lg, in1=tops[:, :, None].to_broadcast([P, PT, E]),
                                op=ALU.is_equal).then_inc(s_route, 1)
                dve.wait_ge(s_route, step + 2)
                v.tensor_tensor(out=is_top[:], in0=is_top[:], in1=numbers, op=ALU.mult).then_inc(s_route, 1)
                dve.wait_ge(s_route, step + 3)
                v.tensor_reduce(first_top[:], is_top[:], AX, ALU.min).then_inc(s_route, 1)
                dve.wait_ge(s_route, step + 4)
                v.tensor_tensor(out=one_hot[:, bass.ds(q * PT, PT), :], in0=numbers,
                                in1=first_top[:, :, None].to_broadcast([P, PT, E]),
                                op=ALU.is_equal).then_inc(s_route, 1)

            v.memset(eps1[:], LN_EPS).then_inc(s_eps, 1)
            v.memset(eps2[:], LN_EPS * X_SCALE ** -2).then_inc(s_eps, 1)
            v.memset(pad_row[:], 0.0).then_inc(s_pad_row, 1)
            dve.wait_ge(s_pad_row, 1)
            v.memset(pad_row[:, 2 * D:2 * D + 1].bitcast(I32), T).then_inc(s_pad_row, 1)
            def router_top():
                dve.wait_ge(s_router, 16)
                v.tensor_reduce(w_max[:, 0:1], router_f[:], AX, ALU.max, apply_absolute_value=True).then_inc(s_wmax, 1)

            def split_router():
                dve.wait_ge(s_small, 16 * SMALL)
                dve.wait_ge(s_const, 16 * 3)
                dve.wait_ge(s_wtop, 1)
                power_of_two(slice(0, 1), 0)
                dve.wait_ge(s_scale, 4)
                v.tensor_scalar(l_scale[:], w_pow[:, 0:1], 1.0 / (X_SCALE * W_SCALE), None, ALU.mult).then_inc(s_scale, 1)
                dve.wait_ge(s_whi, 1)
                v.scalar_tensor_tensor(out=router_split[:, 1, :], in0=router_f[:], scalar=w_mul[:, 0:1],
                                       in1=router_split[:, 0, :], op0=ALU.mult, op1=ALU.subtract).then_inc(s_rlo, 1)

            def split_weights():
                dve.wait_ge(s_w, 48)
                for k in range(3):
                    last = v.tensor_reduce(w_max[:, 1 + k:2 + k], w_full[:, k, :], AX, ALU.max, apply_absolute_value=True)
                last.then_inc(s_wmax, 1)
                dve.wait_ge(s_wtop, 2)
                power_of_two(slice(1, 4), 5)
                dve.wait_ge(s_scale, 9)
                v.tensor_scalar(g_scale[:], w_pow[:, 1:2], 1.0 / (X_SCALE * W_SCALE), None, ALU.mult)
                v.tensor_scalar(h_scale[:], w_inv[:, 1:2], H_SCALE / (X_SCALE * W_SCALE), None, ALU.mult)
                v.tensor_tensor(out=o_scale[:, 1:2], in0=w_pow[:, 1:2], in1=w_pow[:, 2:3], op=ALU.mult).then_inc(s_scale, 1)
                dve.wait_ge(s_scale, 10)
                v.scalar_tensor_tensor(out=o_scale[:, 0:1], in0=o_scale[:, 1:2], scalar=1.0 / (H_SCALE * W_SCALE),
                                       in1=w_pow[:, 3:4], op0=ALU.mult, op1=ALU.mult).then_inc(s_scale, 1)
                for k in range(3):
                    dve.wait_ge(s_whi, 2 + k)
                    v.scalar_tensor_tensor(out=w_split[:, k, 0, 1, :], in0=w_full[:, k, 0:F],
                                           scalar=w_mul[:, 1 + k:2 + k], in1=w_split[:, k, 0, 0, :],
                                           op0=ALU.mult, op1=ALU.subtract).then_inc(s_wlo, 1)
                for q in range(2, PAIRS):
                    dve.wait_ge(s_x[q], 16)

            def pair_step(p, has):
                has(0) and scan(p)
                has(1) and norm1(p + 1)
                has(0) and residual(p)
                has(-1) and split_lo(p - 1)
                has(0) and norm2_scales(p)
                has(2) and norm1_stats(p + 2)
                if isinstance(p, int) and p == -2:
                    router_top()
                if isinstance(p, int) and p == -1:
                    split_router()
                has(-1) and route(p - 1)

            run_pairs(dve, PAIRS, pair_step, between=split_weights)

            def places():
                steps = [0]

                def ready(instruction):
                    instruction.then_inc(s_place, 1)
                    steps[0] += 1
                    dve.wait_ge(s_place, steps[0])

                dve.wait_ge(s_rank, 1)
                by_expert = bank[1][:].rearrange("p (t e) -> p e t", e=E)
                ready(v.tensor_copy(counts[:], by_expert))
                ready(v.tensor_tensor_scan(running[:].rearrange("p e t -> p (e t)"), segment_mask[:],
                                           counts[:].rearrange("p e t -> p (e t)"), 0.0, ALU.mult, ALU.add))
                ready(v.tensor_scalar(tiles_i[:], running[:, :, NT - 1], float(SLOTS - 1), None, ALU.add))
                ready(v.tensor_scalar(tiles_i[:], tiles_i[:], SLOTS.bit_length() - 1, None, ALU.arith_shift_right))
                ready(v.tensor_copy(tiles_f[:], tiles_i[:]))
                ready(v.tensor_tensor_scan(end_tile[:], segment_mask[:, 1:E + 1], tiles_f[:], 0.0, ALU.mult, ALU.add))
                ready(v.tensor_tensor(out=start_row[:], in0=end_tile[:], in1=tiles_f[:], op=ALU.subtract))
                ready(v.tensor_scalar(start_row[:], start_row[:], float(SLOTS), None, ALU.mult))
                ready(v.tensor_tensor(out=running[:], in0=running[:], in1=counts[:], op=ALU.subtract))
                ready(v.tensor_tensor(out=running[:], in0=running[:],
                                      in1=start_row[:, :, None].to_broadcast([P, E, NT]), op=ALU.add))
                ready(v.tensor_tensor(out=running[:], in0=bank[0][:].rearrange("p (t e) -> p e t", e=E),
                                      in1=running[:], op=ALU.add))
                ready(v.tensor_tensor(out=running[:], in0=running[:], in1=one_hot[:].rearrange("p t e -> p e t"),
                                      op=ALU.mult))
                ready(v.tensor_reduce(place_f[:], running[:].rearrange("p e t -> p t e"), AX, ALU.add))
                ready(v.tensor_copy(place[:], place_f[:]))
                ready(v.tensor_tensor(out=ended[:], in0=end_tile[:, None, :].to_broadcast([P, TILES, E]),
                                      in1=tile_number[:, :, None].to_broadcast([P, TILES, E]), op=ALU.is_le))
                ready(v.tensor_reduce(tile_expert_f[:], ended[:], AX, ALU.add))
                ready(v.tensor_scalar(tile_expert_f[:], tile_expert_f[:], 1.0, float(E), ALU.add, ALU.min))
                ready(v.tensor_scalar(tile_weights[:], tile_expert_f[:], float(2 * F), None, ALU.mult))
                assert steps[0] == PLACE_STEPS

            def shared_hidden(s, c):
                dve.wait_ge(s_u, s + 1)
                dve.wait_ge(s_silu, s + 1)
                after(dve, s_hl, s - 1)
                v.scalar_tensor_tensor(out=hid[c], in0=bank[4 + c][:], scalar=h_scale[:, 0:1], in1=silu[c],
                                       op0=ALU.mult, op1=ALU.mult).then_inc(s_hid, 1)

            def shared_lo(s, c, b, k):
                par = k % 2
                dve.wait_ge(s_hh, s + 1)
                after(dve, s_o, b - 1)
                v.tensor_tensor(out=hid_lo[2 * par + c][:], in0=hid[c], in1=hid_hi[2 * par + c][:],
                                op=ALU.subtract).then_inc(s_hl, 1)

            def row_base(b, k, turn):
                after(dve, s_scattered[k], turn * (16 * BT))
                i = bass.ds(b * BT, BT)
                v.tensor_copy(rows[k][:, :, 2 * D].bitcast(I32), ids[:, i])
                v.tensor_copy(row_place[k][:], place[:, i])
                dve.wait_ge(s_o, b + 1)
                v.scalar_tensor_tensor(out=rows[k][:, :, D:2 * D], in0=bank[6 + k % 2][:].rearrange("p (t d) -> p t d", t=BT),
                                       scalar=o_scale[:, 0:1], in1=x1[:, i, :], op0=ALU.mult,
                                       op1=ALU.add).then_inc(s_base, 1)

            def block_step(b, k, turn, has):
                has(-1) and shared_lo(b * FC - 1, 1, b - 1, (k - 1) % 4)
                has(0) and shared_hidden(b * FC, 0)
                has(0) and shared_hidden(b * FC + 1, 1)
                has(0) and shared_lo(b * FC, 0, b, k)
                has(-1) and row_base(b - 1, (k - 1) % 4, turn - (k == 0))

            places()
            dve.wait_ge(s_scale, 11)
            dve.wait_ge(s_wlo_routed, 1)
            for k in range(4):
                v.memset(rows[k][:, :, 2 * D:ROW], 0.0)
            run_blocks(dve, BLOCKS, block_step)

            def tile_lo(j, k):
                dve.wait_ge(s_xh, j + 1)
                after(dve, r_u, j - 2)
                v.tensor_tensor(out=xT_lo[k][:], in0=bank[0][:, 0:SLOTS], in1=xT_hi[k][:],
                                op=ALU.subtract).then_inc(s_xl, 1)

            def routed_hidden(j, k):
                dve.wait_ge(r_u, j + 1)
                dve.wait_ge(r_silu, j + 1)
                after(dve, r_hl, j - 2)
                v.scalar_tensor_tensor(out=hid[k], in0=bank[4 + k][:], scalar=h_scale[:, 0:1], in1=silu[k],
                                       op0=ALU.mult, op1=ALU.mult).then_inc(r_hid, 1)

            def routed_lo(j, k):
                dve.wait_ge(r_hh, j + 1)
                after(dve, r_o, j - 2)
                v.tensor_tensor(out=hid_lo[k][:], in0=hid[k], in1=hid_hi[k][:], op=ALU.subtract).then_inc(r_hl, 1)

            def add_base(j, k, turn):
                dve.wait_ge(s_bin[k], turn * 16 + 16)
                dve.wait_ge(r_o, j + 1)
                after(dve, s_stored[k], turn * (16 * SH))
                v.tensor_copy(result_id[k][:], base_in[k][:, :, D].bitcast(I32))
                v.scalar_tensor_tensor(out=result[k], in0=bank[7][:, 0:SLOTS].rearrange("p (s d) -> p s d", s=SH),
                                       scalar=o_scale[:, 0:1], in1=base_in[k][:, :, 0:D], op0=ALU.mult,
                                       op1=ALU.add).then_inc(r_out, 1)

            run_tiles(dve, TILES, lambda j, k, turn, has: (
                has(1) and tile_lo(j + 1, (k + 1) % 3),
                has(-1) and routed_lo(j - 1, (k - 1) % 3),
                has(0) and routed_hidden(j, k),
                has(-2) and add_base(j - 2, (k - 2) % 3, turn + (k - 2) // 3)))

        @block.gpsimd
        def _(pool):
            g = nc.gpsimd

            def weight_top(cols, n):
                pool.wait_ge(s_wmax, n)
                g.partition_all_reduce(w_top[:, cols], w_max[:, cols], P, MAX_OF_PARTITIONS).then_inc(s_wtop, 1)

            def skip_and_input(q):
                pool.wait_ge(s_n1, q * 2 + 2)
                after(pool, s_x1, q * 2)
                g.tensor_tensor(out=z[:], in0=n1[:], in1=d_bc[:, None, :].to_broadcast([P, PT, D]),
                                op=ALU.mult).then_inc(s_zm, 1)
                pool.wait_ge(s_zm, q + 1)
                g.tensor_tensor(out=z[:], in0=z[:], in1=x1[:, bass.ds(q * PT, PT), :], op=ALU.add).then_inc(s_z, 1)

            weight_top(slice(0, 1), 1)
            pool.wait_ge(s_small, 16 * SMALL)
            run_pairs(pool, PAIRS, lambda p, has: has(1) and skip_and_input(p + 1),
                      between=lambda: weight_top(slice(1, 4), 2))

            pool.wait_ge(s_wlo, 3)
            pool.wait_ge(s_whi, 7)
            for i, k in enumerate((2, 0, 1)):
                full = w_full[:, k, F:]
                g.tensor_tensor(out=full, in0=full, in1=w_mul[:, 1 + k:2 + k].to_broadcast([P, E * F]),
                                op=ALU.mult).then_inc(s_wmul, 1)
                pool.wait_ge(s_wmul, i + 1)
                g.tensor_tensor(out=w_split[:, k, 1:, 1, :], in0=full.rearrange("p (e f) -> p e f", e=E),
                                in1=w_split[:, k, 1:, 0, :], op=ALU.subtract).then_inc(s_wlo_routed, 1)

            def scatter_rows(b, k):
                pool.wait_ge(s_xs, b + 1)
                pool.wait_ge(s_base, b + 1)
                for t in range(BT):
                    g.indirect_dma_start(table[:, :], bass.IndirectOffsetOnAxis(ap=row_place[k][:, t:t + 1], axis=0),
                                         rows[k][:, t, :], None).then_inc(s_scattered[k], 16)

            pool.wait_ge(s_padded, 16 * (PAIRS - 2))
            for b in range(BLOCKS):
                scatter_rows(b, b % 4)

            def scatter_result(j, k):
                pool.wait_ge(r_out, j + 1)
                for s in range(SH):
                    g.indirect_dma_start(
                        out_rows[:, :],
                        bass.IndirectOffsetOnAxis(ap=result_id[k][:, s:s + 1], axis=0),
                        result[k][:, s, :], None, bounds_check=T - 1, oob_is_err=False).then_inc(s_stored[k], 16)

            for j in range(TILES):
                scatter_result(j, j % 3)
            for k in range(3):
                pool.wait_ge(s_stored[k], 16 * SH * (TILES // 3))


def kernel(L0_attn_x, L0_attn_A, L0_attn_B, L0_attn_C, L0_attn_D, L0_ffn_gate_w, L0_ffn_shared_gate,
           L0_ffn_shared_up, L0_ffn_shared_down, L0_ffn_r_gate, L0_ffn_r_up, L0_ffn_r_down):
    import concourse.bacc as bacc
    from concourse.bass_utils import run_bass_kernel_spmd

    x = np.ascontiguousarray(L0_attn_x)
    tokens = x.shape[0] * x.shape[1]
    D = x.shape[2]
    E = L0_ffn_gate_w.shape[0]
    F = L0_ffn_shared_gate.shape[0]

    def with_shared(shared, routed):
        return np.concatenate([np.asarray(shared)[None], np.asarray(routed)], axis=0)

    gate = with_shared(L0_ffn_shared_gate, L0_ffn_r_gate).transpose(2, 0, 1).reshape(D, -1)
    up = with_shared(L0_ffn_shared_up, L0_ffn_r_up).transpose(2, 0, 1).reshape(D, -1)
    down = with_shared(L0_ffn_shared_down, L0_ffn_r_down).reshape(E + 1, D, F // P, P).transpose(3, 0, 2, 1).reshape(P, -1)

    tiles = tokens // SLOTS + E - 1
    token_tiles = tokens // P
    segment_mask = np.ones((E, token_tiles), np.float32)
    segment_mask[:, 0] = 0.0
    row = np.concatenate([np.arange(E) - E, segment_mask.ravel(), np.arange(tiles)]).astype(np.float32)
    consts = np.concatenate([np.eye(P, dtype=np.float32), np.tile(row, (P, 1))], axis=1)
    earlier = np.triu(np.ones((P, P), np.float16), 1)
    token_ids = (np.arange(token_tiles)[None, :] * P + np.arange(P)[:, None]).astype(np.int32)

    arrays = {
        "x": x,
        "bT": np.ascontiguousarray(np.asarray(L0_attn_B).T),
        "cT": np.ascontiguousarray(np.asarray(L0_attn_C).T),
        "a_diag": np.ascontiguousarray(np.diagonal(np.asarray(L0_attn_A))).reshape(-1, 1),
        "d_row": np.asarray(L0_attn_D).reshape(1, -1),
        "gateT": np.ascontiguousarray(np.asarray(L0_ffn_gate_w).T),
        "weights": np.ascontiguousarray(np.stack([gate, up, down])),
        "consts": np.ascontiguousarray(consts),
        "tri_ones": np.concatenate([earlier, np.ones((P, P), np.float16)], axis=1),
        "token_ids": token_ids,
    }
    nc = bacc.Bacc("TRN2", target_bir_lowering=False, num_devices=1)
    args = {n: nc.dram_tensor(f"in_{n}", a.shape, mybir.dt.from_np(a.dtype), kind="ExternalInput").ap()
            for n, a in arrays.items()}
    out = nc.dram_tensor("out", x.shape, F32, kind="ExternalOutput").ap()
    block_kernel(nc, **args, out=out)
    result = run_bass_kernel_spmd(nc, [{f"in_{n}": a for n, a in arrays.items()}], core_ids=[0])
    return result.results[0]["out"]
```
